# Optimizing a Trainium2 kernel written in Bass

```python
import numpy as np
import jax
import jax.numpy as jnp

def _softmax(x, axis=-1):
    return jax.nn.softmax(x, axis=axis)
def _gelu(x):
    return jax.nn.gelu(x, approximate=True)
def _silu(x):
    return jax.nn.silu(x)
def _sigmoid(x):
    return jax.nn.sigmoid(x)
def _layernorm(x, axis=-1, eps=1e-5):
    m = jnp.mean(x, axis=axis, keepdims=True)
    v = jnp.var(x, axis=axis, keepdims=True)
    return (x - m) / jnp.sqrt(v + eps)
def _scatter_add(tgt, idx, src, axis=0):
    return tgt.at[idx].add(src)
def _segment_sum(src, seg, n):
    return jax.ops.segment_sum(src, seg, n)

kernel_name = 'mk_adj_resnorm_d4_adj_128_ca932c'

def setup_inputs(seed: int = 0):
    np.random.seed(seed)
    _w = jnp.asarray
    def _rec_inputs():
        import jax
        import jax.numpy as jnp
        _gk = jax.random.key(seed)
        x = -0.000929 + 1 * jax.random.normal(jax.random.fold_in(_gk, 1), (3327, 128), jnp.float32)
        _a = jax.random.bernoulli(jax.random.fold_in(_gk, 2), 0.00120228, (3327, 3327))
        _a = jnp.logical_or(_a, jnp.swapaxes(_a, -1, -2))
        _a = jnp.logical_or(_a, jnp.eye(3327, dtype=bool))
        _af = _a.astype(jnp.float32)
        _af = _af * jax.random.uniform(jax.random.fold_in(_gk, 3), (3327, 3327), jnp.float32, 0.05, 1)
        adj = _af
        return x, adj
    x, adj = _rec_inputs()
    def _L0_gnn_setup():
        import jax, jax.numpy as jnp
        import numpy as np
        N = 8192
        IN_F = 128
        OUT_F = 128
        key = jax.random.key(seed)
        k1, k2, k3, k4 = jax.random.split(key, 4)
        x = jax.random.normal(k1, (N, IN_F), dtype=jnp.float32)
        adj = jax.random.uniform(k2, (N, N), dtype=jnp.float32)
        lim = 1.0 / np.sqrt(IN_F)
        W = jax.random.uniform(k3, (OUT_F, IN_F), dtype=jnp.float32, minval=-lim, maxval=lim)
        b = jax.random.uniform(k4, (OUT_F,), dtype=jnp.float32, minval=-lim, maxval=lim)
        return {'x': x, 'adj': adj, 'W': W, 'b': b}
    _L0_gnn_all = _L0_gnn_setup()
    _L0_gnn_in = {k: v for k, v in _L0_gnn_all.items() if k in ('W', 'b', )}
    del _L0_gnn_all

    def _L1_gnn_setup():
        import jax, jax.numpy as jnp
        import numpy as np
        N = 1024
        D = 128
        H = 8
        key = jax.random.key(seed)
        ks = jax.random.split(key, 7)
        s = (D * H) ** (-0.5)
        return {'x': jax.random.normal(ks[0], (N, D), dtype=jnp.float32), 'spatial_encoding': jax.random.normal(ks[1], (N, N), dtype=jnp.float32), 'edge_encoding': jax.random.normal(ks[2], (N, N), dtype=jnp.float32), 'Wq': jax.random.normal(ks[3], (D * H, D), dtype=jnp.float32) * s, 'Wk': jax.random.normal(ks[4], (D * H, D), dtype=jnp.float32) * s, 'Wv': jax.random.normal(ks[5], (D * H, D), dtype=jnp.float32) * s, 'Wo': jax.random.normal(ks[6], (D, D * H), dtype=jnp.float32) * s}
    _L1_gnn_all = _L1_gnn_setup()
    _L1_gnn_in = {k: v for k, v in _L1_gnn_all.items() if k in ('Wq', 'Wk', 'Wv', 'Wo', )}
    del _L1_gnn_all

    def _L2_gnn_setup():
        import jax, jax.numpy as jnp
        import numpy as np
        N = 8192
        F = 128
        U = 128
        EDGE_P = 0.002

        def adj_norm(adj):
            a_hat = adj + jnp.eye(adj.shape[0], dtype=adj.dtype)
            d_inv_sqrt = jax.lax.rsqrt(jnp.sum(a_hat, axis=-1))
            return a_hat * d_inv_sqrt[:, None] * d_inv_sqrt[None, :]
        key = jax.random.key(seed)
        k1, k2, k3 = jax.random.split(key, 3)
        a = (jax.random.uniform(k1, (N, N)) < EDGE_P).astype(jnp.float32)
        adj = jnp.maximum(a, a.T)
        x = jax.random.normal(k2, (N, F), dtype=jnp.float32)
        W = jax.random.normal(k3, (F, U), dtype=jnp.float32) * 0.05
        b = jnp.zeros((U,), dtype=jnp.float32)
        return {'x': x, 'adj': adj, 'W': W, 'b': b}
    _L2_gnn_all = _L2_gnn_setup()
    _L2_gnn_in = {k: v for k, v in _L2_gnn_all.items() if k in ('W', 'b', )}
    del _L2_gnn_all

    def _L3_gnn_setup():
        import jax, jax.numpy as jnp
        import numpy as np
        N = 8192
        IN_DIM = 128
        OUT_DIM = 128
        DENSITY = 0.01
        key = jax.random.key(seed)
        kx, ka, kw, ks, kd = jax.random.split(key, 5)
        x = jax.random.normal(kx, (N, IN_DIM), dtype=jnp.float32) * 0.1
        adj_matrix = (jax.random.uniform(ka, (N, N)) < DENSITY).astype(jnp.float32)
        adj_matrix = jnp.maximum(adj_matrix, jnp.eye(N, dtype=jnp.float32))
        weight = jax.random.normal(kw, (OUT_DIM, IN_DIM), dtype=jnp.float32) * 0.05
        att_src = jax.random.normal(ks, (1, OUT_DIM), dtype=jnp.float32) * 0.1
        att_dst = jax.random.normal(kd, (1, OUT_DIM), dtype=jnp.float32) * 0.1
        return {'x': x, 'adj_matrix': adj_matrix, 'weight': weight, 'att_src': att_src, 'att_dst': att_dst}
    _L3_gnn_all = _L3_gnn_setup()
    _L3_gnn_in = {k: v for k, v in _L3_gnn_all.items() if k in ('weight', 'att_src', 'att_dst', )}
    del _L3_gnn_all

    return {
        "x": x,
        "adj": adj,
        "L0_gnn_W": _L0_gnn_in["W"],
        "L0_gnn_b": _L0_gnn_in["b"],
        "L1_gnn_Wq": _L1_gnn_in["Wq"],
        "L1_gnn_Wk": _L1_gnn_in["Wk"],
        "L1_gnn_Wv": _L1_gnn_in["Wv"],
        "L1_gnn_Wo": _L1_gnn_in["Wo"],
        "L2_gnn_W": _L2_gnn_in["W"],
        "L2_gnn_b": _L2_gnn_in["b"],
        "L3_gnn_weight": _L3_gnn_in["weight"],
        "L3_gnn_att_src": _L3_gnn_in["att_src"],
        "L3_gnn_att_dst": _L3_gnn_in["att_dst"],
    }

def reference(x, adj, L0_gnn_W, L0_gnn_b, L1_gnn_Wq, L1_gnn_Wk, L1_gnn_Wv, L1_gnn_Wo, L2_gnn_W, L2_gnn_b, L3_gnn_weight, L3_gnn_att_src, L3_gnn_att_dst):
    import jax
    import jax.numpy as jnp
    def _L0_gnn_ref(x, adj, W, b):
        import jax, jax.numpy as jnp
        import numpy as np
        N = 8192
        IN_F = 128
        OUT_F = 128
        h = x @ W.T + b
        a = adj + jnp.eye(adj.shape[0], dtype=adj.dtype)
        rowsum = a.sum(axis=1)
        r_inv_sqrt = jnp.where(rowsum > 0, rowsum ** (-0.5), 0.0)
        a_norm = a * r_inv_sqrt[:, None] * r_inv_sqrt[None, :]
        return a_norm @ h

    def _L1_gnn_ref(x, spatial_encoding, edge_encoding, Wq, Wk, Wv, Wo):
        import jax, jax.numpy as jnp
        import numpy as np
        N = 1024
        D = 128
        H = 8
        n, d = x.shape
        h = Wq.shape[0] // d
        scale = d ** (-0.5)
        q = (x @ Wq.T).reshape(d, n, h)
        k = (x @ Wk.T).reshape(d, n, h)
        v = (x @ Wv.T).reshape(d, n, h)
        a = jnp.einsum('dnh,dmh->dnm', q, k) * scale
        a = a + spatial_encoding + edge_encoding
        a = jax.nn.softmax(a, axis=2)
        out = jnp.einsum('dnm,dmh->dnh', a, v)
        out = out.reshape(n, h * d)
        return out @ Wo.T

    def _L2_gnn_ref(x, adj, W, b):
        import jax, jax.numpy as jnp
        import numpy as np
        N = 8192
        F = 128
        U = 128
        EDGE_P = 0.002

        def adj_norm(adj):
            a_hat = adj + jnp.eye(adj.shape[0], dtype=adj.dtype)
            d_inv_sqrt = jax.lax.rsqrt(jnp.sum(a_hat, axis=-1))
            return a_hat * d_inv_sqrt[:, None] * d_inv_sqrt[None, :]
        adj_n = adj_norm(adj)
        h = adj_n @ x
        h = h @ W + b
        return jax.nn.relu(h)

    def _L3_gnn_ref(x, adj_matrix, weight, att_src, att_dst):
        import jax, jax.numpy as jnp
        import numpy as np
        N = 8192
        IN_DIM = 128
        OUT_DIM = 128
        DENSITY = 0.01
        H = x @ weight.T
        alpha_src = jnp.sum(H * att_src[0], axis=-1)
        alpha_dst = jnp.sum(H * att_dst[0], axis=-1)
        C = alpha_src[None, :] + alpha_dst[:, None]
        Tau = adj_matrix.T * jnp.exp(jnp.maximum(0.2 * C, C))
        att_weights = Tau / jnp.sum(Tau, axis=1, keepdims=True)
        Z = adj_matrix.T * att_weights @ H
        return Z

    x = _layernorm(x + _L0_gnn_ref(x, adj, L0_gnn_W, L0_gnn_b), axis=-1)
    x = _layernorm(x + _L1_gnn_ref(x, adj, adj, L1_gnn_Wq, L1_gnn_Wk, L1_gnn_Wv, L1_gnn_Wo), axis=-1)
    x = _layernorm(x + _L2_gnn_ref(x, adj, L2_gnn_W, L2_gnn_b), axis=-1)
    x = _layernorm(x + _L3_gnn_ref(x, adj, L3_gnn_weight, L3_gnn_att_src, L3_gnn_att_dst), axis=-1)
    return x


_drawn_inputs = setup_inputs


def setup_inputs(seed=0):
    import zlib

    import numpy as np

    out = dict(_drawn_inputs(seed))
    spreads = {'L2_gnn_b': (0.0, 0.1)}
    factors = {'L1_gnn_Wq': 8.0, 'L1_gnn_Wk': 8.0, 'L1_gnn_Wv': 8.0, 'L1_gnn_Wo': 8.0}
    for name, (base, spread) in spreads.items():
        noise = np.random.default_rng([zlib.crc32(name.encode()), seed]).standard_normal(out[name].shape)
        drawn = base * np.exp(spread * noise) if base else spread * noise
        out[name] = jnp.asarray(drawn.astype(out[name].dtype))
    for name, factor in factors.items():
        out[name] = (out[name] * factor).astype(out[name].dtype)
    return out
```

```python
from contextlib import ExitStack

import concourse.bass as bass
from concourse import mybir

F32 = mybir.dt.float32
BF16 = mybir.dt.bfloat16
ALU = mybir.AluOpType
ACT = mybir.ActivationFunctionType
AX = mybir.AxisListType

P = 128
N = 3327
F = 128
BLOCKS = -(-N // P)
NP = BLOCKS * P
FULL = BLOCKS * (P - 1)
HALF = BLOCKS // 2
HEADS = 8
BATCHES = 128
QCOLS = HEADS * F
QGROUPS = QCOLS // HEADS
VG = HEADS + 1
SCALE = float(F) ** -0.5
EPS = 1e-5
BANK = 512
SPLITS = 3
SROW = 32
SHIFT0 = SPLITS * HEADS
KROWS = SPLITS * SROW
PREP = P // SROW
LOAD = 16
CHUNK_GROUPS = ((0, 2, 7), (14, 2, 6))
SBUFS = 3
ADJ_PARTS = ((0, 7), (7, 13), (13, 19), (19, BLOCKS))
FINISH_AT = 9
POOL_LAG = 4
HIGH, BOUND, ADJ_BOUND = 30.0, 40.0, 5.0
ROUND = 1.0001
POOL_BLOCKS = (1, 4, 7, 10, 13, 17, 20, 23)


class Chain:

    def __init__(self, eng, sem):
        self.eng, self.sem, self.n = eng, sem, 0

    def __call__(self, ins):
        self.n += 1
        ins.then_inc(self.sem, 1)
        self.eng.wait_ge(self.sem, self.n)


class Memory:
    def __init__(self, nc, stack):
        self.nc, self.stack, self.used = nc, stack, []
        stack.callback(self.clear)

    def clear(self):
        if self.used:
            self.nc.clear_and_free_semaphores(self.used)
            self.nc.all_engine_barrier()

    def sb(self, name, shape, dt=F32):
        return self.stack.enter_context(self.nc.sbuf_tensor(name, list(shape), dt))

    def sem(self, name):
        self.used.append(self.nc.alloc_semaphore(name))
        return self.used[-1]

    def sems(self, name, n):
        return [self.sem(f"{name}{k}") for k in range(n)]


def bcast(ap, n):
    p, a = ap.shape
    return ap.unsqueeze(2).to_broadcast([p, a, n])


def inverse_root(nc, link, root, tmp, value):
    v = nc.vector
    link(v.reciprocal(root, root))
    link(v.tensor_tensor(tmp, root, root, ALU.mult))
    link(v.tensor_tensor(tmp, tmp, value, ALU.mult))
    link(v.tensor_scalar(tmp, tmp, -0.5, 1.5, ALU.mult, ALU.add))
    link(v.tensor_tensor(root, root, tmp, ALU.mult))


def layer_norm(nc, dve, link, x, sq, norm):
    v = nc.vector
    stat, tmp, rstd = norm.stat, norm.tmp, norm.rstd
    link(v.reduce_sum(stat[:, :], x[:, :, :], AX.X))
    link(v.tensor_scalar(stat[:, :], stat[:, :], 1.0 / F, None, ALU.mult))
    link(v.tensor_tensor(x[:, :, :], x[:, :, :], bcast(stat[:, :], F), ALU.subtract))
    link(v.tensor_tensor(sq[:, :, :], x[:, :, :], x[:, :, :], ALU.mult))
    link(v.reduce_sum(stat[:, :], sq[:, :, :], AX.X))
    v.tensor_scalar(stat[:, :], stat[:, :], 1.0 / F, EPS, ALU.mult, ALU.add).then_inc(norm.var_ready, 1)
    dve.wait_ge(norm.root_ready, 1)
    inverse_root(nc, link, rstd[:, :], tmp[:, :], stat[:, :])
    v.tensor_tensor(x[:, :, :], x[:, :, :], bcast(rstd[:, :], F), ALU.mult).then_inc(norm.done, 1)


def layer_norm_root(nc, act, norm):
    act.wait_ge(norm.var_ready, 1)
    nc.scalar.activation(norm.rstd[:, :], norm.stat[:, :], ACT.Sqrt).then_inc(norm.root_ready, 1)


class Norm:

    def __init__(self, mem, name):
        self.stat, self.tmp, self.rstd = (mem.sb(f"{name}_{x}", [P, BLOCKS]) for x in ("stat", "tmp", "rstd"))
        self.var_ready, self.root_ready, self.done = (mem.sem(f"{name}_{x}") for x in (
            "var_ready", "root_ready", "norm_done"))


def setup_phase(nc, keep, x_in, b0, b2, att_src, att_dst, o_flat):
    with ExitStack() as stack:
        mem = Memory(nc, stack)
        zeros = mem.sb("zeros", [1, QCOLS])
        zeroed, ident_made, loaded = mem.sem("zeroed"), mem.sem("ident_made"), mem.sem("setup_loaded")
        block = stack.enter_context(nc.Block())

        @block.gpsimd
        def _(pool):
            nc.gpsimd.memset(keep.ident[:, :], 0.0).then_inc(ident_made, 1)
            pool.wait_ge(ident_made, 1)
            nc.gpsimd.affine_select(out=keep.ident[:, :], in_=keep.ident[:, :], compare_op=ALU.not_equal,
                                    fill=1.0, base=0, pattern=[[-1, P]],
                                    channel_multiplier=1).then_inc(ident_made, 1)
            pool.wait_ge(ident_made, 2)
            nc.gpsimd.tensor_copy(keep.ident16[:, :], keep.ident[:, :])

        @block.vector
        def _(dve):
            nc.vector.memset(keep.x[96:P, BLOCKS - 1, :], 0.0).then_inc(zeroed, 1)
            nc.vector.memset(zeros[:, :], 0.0).then_inc(zeroed, 1)
            nc.vector.memset(keep.ones[:, :], 1.0)

        @block.sync
        def _(sp):
            rows = x_in[0:FULL].rearrange("(p i) f -> p i f", i=BLOCKS)
            sp.dma_start(keep.bias0[:, :], b0.partition_broadcast(P)).then_inc(loaded, LOAD)
            sp.dma_start(keep.bias2[:, :], b2.partition_broadcast(P)).then_inc(loaded, LOAD)
            sp.dma_start(keep.att_src[:, :], att_src[0].partition_broadcast(P)).then_inc(loaded, LOAD)
            sp.dma_start(keep.att_dst[:, :], att_dst.rearrange("a f -> f a")).then_inc(loaded, LOAD)
            sp.wait_ge(zeroed, 2)
            sp.dma_start(keep.x[0:112], rows[0:112]).then_inc(loaded, LOAD)
            sp.dma_start(keep.x[112:127], rows[112:127]).then_inc(loaded, LOAD)
            sp.dma_start(keep.x[127:P, 0:BLOCKS - 1], x_in[FULL:N].rearrange("(p i) f -> p i f", p=1)
                         ).then_inc(loaded, LOAD)
            sp.dma_start(o_flat[N * QCOLS:NP * QCOLS].unsqueeze(0), zeros[:, :]).then_inc(loaded, LOAD)
            sp.wait_ge(loaded, 8 * LOAD)


def adjacency_phase(nc, keep, adj, adj_t):
    regular = adj[0:FULL].rearrange("(p i) m -> i p m", i=BLOCKS)
    last = adj[FULL:N].rearrange("(i p) m -> i p m", p=1)
    flat_t = adj_t.rearrange("i p j q -> i p (j q)")
    with ExitStack() as stack:
        mem = Memory(nc, stack)
        nat = [mem.sb(f"nat{b}", [P, NP]) for b in range(2)]
        tr = [mem.sb(f"tr{b}", [P, NP]) for b in range(2)]
        positive, floor, tmp = (mem.sb("row_" + x, [P, BLOCKS]) for x in ("positive", "floor", "tmp"))
        degrees, roots = mem.sem("degrees"), mem.sem("roots")
        loaded = mem.sems("adj_loaded", 2)
        padded, summed = mem.sem("adj_padded"), mem.sem("adj_summed")
        turned = mem.sems("half_turned", 2)
        copied = mem.sems("half_copied", 2)
        stored = mem.sems("adj_stored", 2)
        chain = mem.sem("adj_chain")
        block = stack.enter_context(nc.Block())

        @block.sync
        def _(sp):
            def load(i, b, whole=True):
                sp.dma_start(nat[b][0:112, 0:N], regular[i, 0:112]).then_inc(loaded[b], LOAD)
                sp.dma_start(nat[b][112:127, 0:N], regular[i, 112:127]).then_inc(loaded[b], LOAD)
                if whole:
                    sp.dma_start(nat[b][127:P, 0:N], last[i]).then_inc(loaded[b], LOAD)

            def free(i):
                sp.wait_ge(turned[1], i - 1)
                sp.wait_ge(summed, i - 1)

            def store(i, b):
                for h in range(2):
                    sp.wait_ge(copied[h], i + 1)
                sp.dma_start(flat_t[i], tr[b][:, :]).then_inc(stored[b], LOAD)

            load(0, 0)
            load(1, 1)
            with sp.Fori(0, BLOCKS // 2 - 2) as t:
                for b in range(2):
                    store(2 * t + b, b)
                    free(2 * t + b + 2)
                    load(2 * t + b + 2, b)
            store(BLOCKS - 4, 0)
            free(BLOCKS - 2)
            load(BLOCKS - 2, 0)
            store(BLOCKS - 3, 1)
            free(BLOCKS - 1)
            sp.wait_ge(padded, 3)
            load(BLOCKS - 1, 1, whole=False)
            store(BLOCKS - 2, 0)
            store(BLOCKS - 1, 1)
            for b in range(2):
                sp.wait_ge(stored[b], LOAD * BLOCKS // 2)

        @block.tensor
        def _(pe):
            def turn(i, t, b, parts):
                if parts == 3:
                    pe.wait_ge(loaded[b], (t + 1) * (3 * LOAD))
                else:
                    pe.wait_ge(loaded[b], t * 3 * LOAD + parts * LOAD)
                for h in range(2):
                    pe.wait_ge(copied[h], i)
                    for j in range(HALF * h, HALF * (h + 1)):
                        col = 2048 * h + P * (j - HALF * h)
                        ins = nc.tensor.transpose(keep.ps[:, col:col + P], nat[b][:, j:j + FULL + 1:BLOCKS],
                                                  keep.ident[:, :])
                    ins.then_inc(turned[h], 1)

            pe.wait_ge(padded, 2)
            with pe.Fori(0, BLOCKS // 2 - 1) as t:
                for b in range(2):
                    turn(2 * t + b, t, b, 3)
            turn(BLOCKS - 2, BLOCKS // 2 - 1, 0, 3)
            turn(BLOCKS - 1, BLOCKS // 2 - 1, 1, 2)

        @block.scalar
        def _(act):
            with act.Fori(0, BLOCKS // 2) as t:
                for b in range(2):
                    act.wait_ge(stored[b], t * LOAD)
                    for h in range(2):
                        act.wait_ge(turned[h], 2 * t + b + 1)
                        nc.scalar.activation(tr[b][:, HALF * P * h:HALF * P * (h + 1)],
                                             keep.ps[:, 2048 * h:2048 * h + HALF * P],
                                             ACT.Copy).then_inc(copied[h], 1)
            act.wait_ge(degrees, 1)
            nc.scalar.activation(keep.deg2[:, :], keep.rowsum[:, :], ACT.Sqrt).then_inc(roots, 1)
            act.wait_ge(degrees, 2)
            nc.scalar.activation(keep.deg0[:, :], floor[:, :], ACT.Sqrt).then_inc(roots, 1)

        @block.vector
        def _(dve):
            def row_sum(i, t, b, parts):
                if parts == 3:
                    dve.wait_ge(loaded[b], (t + 1) * (3 * LOAD))
                else:
                    dve.wait_ge(loaded[b], t * 3 * LOAD + parts * LOAD)
                nc.vector.reduce_sum(keep.rowsum[:, bass.ds(i, 1)], nat[b][:, 0:N], AX.X)
                nc.vector.tensor_reduce(keep.absmax[:, bass.ds(i, 1)], nat[b][:, 0:N], axis=AX.X, op=ALU.max,
                                        apply_absolute_value=True).then_inc(summed, 1)

            link = Chain(dve, chain)
            for b in range(2):
                nc.vector.memset(nat[b][:, N:NP], 0.0).then_inc(padded, 1)
            with dve.Fori(0, BLOCKS // 2 - 1) as t:
                for b in range(2):
                    row_sum(2 * t + b, t, b, 3)
            dve.wait_ge(turned[1], BLOCKS - 2)
            dve.wait_ge(summed, BLOCKS - 2)
            nc.vector.memset(nat[1][96:P, :], 0.0).then_inc(padded, 1)
            row_sum(BLOCKS - 2, BLOCKS // 2 - 1, 0, 3)
            row_sum(BLOCKS - 1, BLOCKS // 2 - 1, 1, 2)
            dve.wait_ge(summed, BLOCKS)
            nc.vector.tensor_scalar(keep.rowsum[:, :], keep.rowsum[:, :], 1.0, None, ALU.add).then_inc(degrees, 1)
            dve.wait_ge(degrees, 1)
            link(nc.vector.tensor_scalar(positive[:, :], keep.rowsum[:, :], 0.0, None, ALU.is_gt))
            nc.vector.tensor_scalar(floor[:, :], keep.rowsum[:, :], 1e-30, None, ALU.max).then_inc(degrees, 1)
            dve.wait_ge(roots, 2)
            inverse_root(nc, link, keep.deg2[:, :], tmp[:, :], keep.rowsum[:, :])
            inverse_root(nc, link, keep.deg0[:, :], tmp[:, :], floor[:, :])
            link(nc.vector.tensor_tensor(keep.deg0[:, :], keep.deg0[:, :], positive[:, :], ALU.mult))


def gcn_phase(nc, keep, adj_t, weight, deg, bias, inner):
    flat_t = adj_t.rearrange("i p j q -> i p (j q)")
    name = "g0" if inner else "g2"
    x = keep.x
    with ExitStack() as stack:
        mem = Memory(nc, stack)
        w = mem.sb(name + "w", [P, F])
        w_t = mem.sb(name + "w_t", [P, F])
        x_t = mem.sb(name + "x_t", [P, BLOCKS, P])
        z = mem.sb(name + "z", [P, BLOCKS, F])
        tile = [mem.sb(f"{name}tile{b}", [P, BLOCKS, P]) for b in range(2)]
        tmp = [mem.sb(f"{name}tmp{b}", [P, F]) for b in range(2)]
        norm = Norm(mem, name)
        w_loaded, turned, copied = mem.sem(name + "w_loaded"), mem.sem(name + "turned"), mem.sem(name + "copied")
        projected, z_ready = mem.sem(name + "projected"), mem.sem(name + "z_ready")
        loaded, acc_ready = mem.sems(name + "loaded", 2), mem.sems(name + "acc_ready", 2)
        added, scaled, done = mem.sems(name + "added", 2), mem.sems(name + "scaled", 2), mem.sems(name + "done", 2)
        chain = mem.sem(name + "chain")
        ps = keep.ps
        w_col = NP
        acc = [ps[:, BANK * b:BANK * b + F] for b in range(2)]
        block = stack.enter_context(nc.Block())

        @block.sync
        def _(sp):
            sp.dma_start(w[:, :], weight).then_inc(w_loaded, LOAD)
            with sp.Fori(0, BLOCKS // 2) as t:
                for b in range(2):
                    sp.wait_ge(acc_ready[b], t)
                    sp.dma_start(tile[b][:, :, :].rearrange("p j q -> p (j q)"),
                                 flat_t[2 * t + b]).then_inc(loaded[b], LOAD)

        @block.tensor
        def _(pe):
            for i in range(BLOCKS):
                nc.tensor.transpose(ps[:, P * i:P * (i + 1)], x[:, i, :], keep.ident[:, :]).then_inc(turned, 1)
            if inner:
                pe.wait_ge(w_loaded, LOAD)
                nc.tensor.transpose(ps[:, w_col:w_col + F], w[:, :], keep.ident[:, :]).then_inc(turned, 1)
            pe.wait_ge(copied, 2)
            if not inner:
                pe.wait_ge(w_loaded, LOAD)
            rhs = w_t if inner else w
            for i in range(BLOCKS):
                ins = nc.tensor.matmul(ps[:, P * i:P * (i + 1)], x_t[:, i, :], rhs[:, :], start=True, stop=True)
            ins.then_inc(projected, 1)
            pe.wait_ge(z_ready, 1)
            with pe.Fori(0, BLOCKS // 2) as t:
                for b in range(2):
                    pe.wait_ge(loaded[b], (t + 1) * LOAD)
                    pe.wait_ge(added[b], t)
                    for j in range(BLOCKS):
                        ins = nc.tensor.matmul(acc[b], tile[b][:, j, :], z[:, j, :],
                                               start=j == 0, stop=j == BLOCKS - 1)
                    ins.then_inc(acc_ready[b], 1)

        @block.vector
        def _(dve):
            v = nc.vector
            link = Chain(dve, chain)
            dve.wait_ge(turned, BLOCKS + inner)
            v.tensor_copy(x_t[:, :, :].rearrange("p i q -> p (i q)"), ps[:, 0:NP]).then_inc(copied, 1)
            if inner:
                v.tensor_copy(w_t[:, :], ps[:, w_col:w_col + F]).then_inc(copied, 1)
            else:
                v.memset(w_t[:, :], 0.0).then_inc(copied, 1)
            dve.wait_ge(projected, 1)
            xw = ps[:, 0:NP].rearrange("p (i f) -> p i f", f=F)
            if inner:
                link(v.tensor_tensor(z[:, :, :], xw, bias[:, :].unsqueeze(1).to_broadcast([P, BLOCKS, F]), ALU.add))
                v.tensor_tensor(z[:, :, :], z[:, :, :], bcast(deg[:, :], F), ALU.mult).then_inc(z_ready, 1)
            else:
                v.tensor_tensor(z[:, :, :], xw, bcast(deg[:, :], F), ALU.mult).then_inc(z_ready, 1)
            dve.wait_ge(z_ready, 1)
            with dve.Fori(0, BLOCKS // 2) as t:
                for b in range(2):
                    i = bass.ds(2 * t + b, 1)
                    x_i = x[:, i, :].rearrange("p a f -> p (a f)")
                    dve.wait_ge(acc_ready[b], t + 1)
                    dve.wait_ge(done[b], t)
                    v.tensor_tensor(tmp[b][:, :], acc[b], z[:, i, :].rearrange("p a f -> p (a f)"),
                                    ALU.add).then_inc(added[b], 1)
                    dve.wait_ge(added[b], t + 1)
                    if inner:
                        v.scalar_tensor_tensor(out=x_i, in0=tmp[b][:, :], scalar=deg[:, i], in1=x_i,
                                               op0=ALU.mult, op1=ALU.add).then_inc(done[b], 1)
                    else:
                        v.scalar_tensor_tensor(out=tmp[b][:, :], in0=tmp[b][:, :], scalar=deg[:, i],
                                               in1=bias[:, :], op0=ALU.mult, op1=ALU.add).then_inc(scaled[b], 1)
                        dve.wait_ge(scaled[b], t + 1)
                        v.scalar_tensor_tensor(out=x_i, in0=tmp[b][:, :], scalar=0.0, in1=x_i,
                                               op0=ALU.max, op1=ALU.add).then_inc(done[b], 1)
            for b in range(2):
                dve.wait_ge(done[b], BLOCKS // 2)
            layer_norm(nc, dve, link, x, z, norm)

        @block.scalar
        def _(act):
            layer_norm_root(nc, act, norm)


def qkv_phase(nc, keep, wq, wk, wv, q_flat, k_flat, v_flat):
    weights = (wq, wk, wv)
    with ExitStack() as stack:
        mem = Memory(nc, stack)
        w = mem.sb("wqkv", [P, 3, QCOLS // P, F])
        w_t = mem.sb("wqkv_t", [P, 3, QCOLS])
        x_t = mem.sb("qkv_x_t", [P, BLOCKS, P])
        x_i = [mem.sb(f"qkv_x_i{b}", [P, P]) for b in range(2)]
        q = [mem.sb(f"q_rows{b}", [P, QCOLS]) for b in range(2)]
        k = [mem.sb(f"k_rows{b}", [P, QCOLS]) for b in range(2)]
        v = [mem.sb(f"v_rows{b}", [P, QGROUPS, VG]) for b in range(2)]
        w_loaded, x_turned, w_turned = mem.sem("wqkv_loaded"), mem.sem("qkv_x_turned"), mem.sem("wqkv_turned")
        x_copied, w_copied = mem.sem("qkv_x_copied"), mem.sem("wqkv_copied")
        x_ready = mem.sems("qkv_x_ready", 2)
        q_done, k_done, v_done = mem.sem("q_done"), mem.sem("k_done"), mem.sem("v_done")
        q_copied, k_copied, v_copied = mem.sem("q_copied"), mem.sem("k_copied"), mem.sem("v_copied")
        ones_set, stored = mem.sem("v_ones_set"), mem.sems("qkv_stored", 2)
        ps = keep.ps
        block = stack.enter_context(nc.Block())

        @block.sync
        def _(sp):
            for n, weight in enumerate(weights):
                sp.dma_start(w[:, n], weight.rearrange("(c o) f -> o c f", o=P)).then_inc(w_loaded, LOAD)
            q_rows = q_flat.rearrange("(p i c) -> i p c", i=BLOCKS, c=QCOLS)
            k_rows = k_flat.rearrange("(p i c) -> i p c", i=BLOCKS, c=QCOLS)
            v_rows = v_flat.rearrange("(p i c) -> i p c", i=BLOCKS, c=QGROUPS * VG)
            with sp.Fori(0, BLOCKS // 2) as t:
                for b in range(2):
                    i = 2 * t + b
                    sp.wait_ge(q_copied, i + 1)
                    sp.dma_start(q_rows[i], q[b][:, :]).then_inc(stored[b], LOAD)
                    sp.wait_ge(k_copied, i + 1)
                    sp.dma_start(k_rows[i], k[b][:, :]).then_inc(stored[b], LOAD)
                    sp.wait_ge(v_copied, i + 1)
                    sp.dma_start(v_rows[i], v[b][:, :, :].rearrange("p g h -> p (g h)")).then_inc(stored[b], LOAD)
            for b in range(2):
                sp.wait_ge(stored[b], 3 * LOAD * (BLOCKS // 2))

        @block.tensor
        def _(pe):
            for i in range(BLOCKS):
                ins = nc.tensor.transpose(ps[:, P * i:P * (i + 1)], keep.x[:, i, :], keep.ident[:, :])
            ins.then_inc(x_turned, 1)
            pe.wait_ge(w_loaded, 3 * LOAD)
            pe.wait_ge(x_copied, 2)
            for n in range(3):
                for c in range(QCOLS // P):
                    col = QCOLS * n + P * c
                    ins = nc.tensor.transpose(ps[:, col:col + P], w[:, n, c, :], keep.ident[:, :])
            ins.then_inc(w_turned, 1)
            pe.wait_ge(w_copied, 1)
            with pe.Fori(0, BLOCKS // 2) as t:
                for b in range(2):
                    i = 2 * t + b
                    pe.wait_ge(x_ready[b], t + 1)
                    for n, (done, copied) in enumerate(((q_done, q_copied), (k_done, k_copied), (v_done, v_copied))):
                        pe.wait_ge(copied, i)
                        for c in range(0, QCOLS, BANK):
                            ins = nc.tensor.matmul(ps[:, QCOLS * n + c:QCOLS * n + c + BANK], x_i[b][:, :],
                                                   w_t[:, n, c:c + BANK], start=True, stop=True)
                        ins.then_inc(done, 1)

        @block.scalar
        def _(act):
            act.wait_ge(x_copied, 2)
            with act.Fori(0, BLOCKS // 2) as t:
                for b in range(2):
                    i = 2 * t + b
                    act.wait_ge(v_done, 2 * t)
                    nc.scalar.activation(x_i[b][:, :], x_t[:, bass.ds(i, 1), :].rearrange("p a q -> p (a q)"),
                                         ACT.Copy).then_inc(x_ready[b], 1)
                for b in range(2):
                    i = 2 * t + b
                    act.wait_ge(stored[b], t * (3 * LOAD))
                    act.wait_ge(q_done, i + 1)
                    nc.scalar.activation(q[b][:, :], ps[:, 0:QCOLS], ACT.Copy).then_inc(q_copied, 1)

        @block.vector
        def _(dve):
            for b in range(2):
                nc.vector.memset(v[b][:, :, HEADS:VG], 1.0).then_inc(ones_set, 1)
            dve.wait_ge(x_turned, 1)
            flat_x = x_t[:, :, :].rearrange("p i q -> p (i q)")
            nc.vector.memset(flat_x[:, N:NP], 0.0).then_inc(x_copied, 1)
            nc.vector.tensor_copy(flat_x[:, 0:N], ps[:, 0:N]).then_inc(x_copied, 1)
            dve.wait_ge(w_turned, 1)
            nc.vector.tensor_copy(w_t[:, :, :].rearrange("p n c -> p (n c)"), ps[:, 0:3 * QCOLS]).then_inc(w_copied, 1)
            dve.wait_ge(ones_set, 2)
            with dve.Fori(0, BLOCKS // 2) as t:
                for b in range(2):
                    i = 2 * t + b
                    dve.wait_ge(stored[b], t * (3 * LOAD))
                    dve.wait_ge(k_done, i + 1)
                    nc.vector.tensor_copy(k[b][:, :], ps[:, QCOLS:2 * QCOLS]).then_inc(k_copied, 1)
                    dve.wait_ge(v_done, i + 1)
                    nc.vector.tensor_copy(v[b][:, :, 0:HEADS],
                                          ps[:, 2 * QCOLS:3 * QCOLS].rearrange("p (g h) -> p g h", h=HEADS)
                                          ).then_inc(v_copied, 1)


def split_phase(nc, keep, flat, parts_t, norms, name, shift_row):
    batch = HEADS * N
    folded = bass.AP(flat.tensor, 0, [[PREP * batch, BATCHES // PREP], [BLOCKS * HEADS, P], [batch, PREP],
                                      [1, BLOCKS * HEADS]])
    stores = parts_t.rearrange("(g d) r n -> g (d r) n", d=PREP)
    with ExitStack() as stack:
        mem = Memory(nc, stack)
        raw = [mem.sb(f"{name}raw{b}", [P, PREP, BLOCKS, HEADS]) for b in range(2)]
        rest = [mem.sb(f"{name}rest{b}", [P, PREP, BLOCKS, HEADS]) for b in range(2)]
        parts = [mem.sb(f"{name}parts{b}", [P, BLOCKS, PREP, SROW], BF16) for b in range(2)]
        out = [mem.sb(f"{name}out{b}", [P, NP], BF16) for b in range(2)]
        square = [mem.sb(f"{name}square{b}", [P, PREP * BLOCKS, HEADS]) for b in range(2)]
        padded = mem.sem(name + "padded")
        squared, normed = mem.sems(name + "squared", 2), mem.sems(name + "normed", 2)
        loaded, first, rested = mem.sems(name + "loaded", 2), mem.sems(name + "first", 2), mem.sems(name + "rested", 2)
        second, split = mem.sems(name + "second", 2), mem.sems(name + "split", 2)
        turned, copied_a = mem.sems(name + "turned", 2), mem.sems(name + "copied_a", 2)
        copied_v, stored = mem.sems(name + "copied_v", 2), mem.sems(name + "stored", 2)
        ps16 = keep.ps[:, :].bitcast(BF16)
        half = 4 * BANK
        steps = BATCHES // PREP // 2

        def part(b, s):
            return parts[b][:, :, :, HEADS * s:HEADS * (s + 1)].rearrange("p i d h -> p d i h")

        block = stack.enter_context(nc.Block())

        @block.sync
        def _(sp):
            def store(t, b):
                sp.wait_ge(copied_a[b], t + 1)
                sp.wait_ge(copied_v[b], t + 1)
                sp.dma_start(stores[2 * t + b], out[b][:, :]).then_inc(stored[b], LOAD)

            def load(t, b):
                sp.wait_ge(rested[b], t)
                sp.wait_ge(squared[b], t)
                sp.dma_start(raw[b][:, :, :, :].rearrange("p d i h -> p d (i h)"),
                             folded[2 * t + b]).then_inc(loaded[b], LOAD)

            for t in range(2):
                for b in range(2):
                    load(t, b)
            with sp.Fori(0, steps - 2) as t:
                for b in range(2):
                    load(t + 2, b)
                    store(t, b)
            for t in (steps - 2, steps - 1):
                for b in range(2):
                    store(t, b)
            for b in range(2):
                sp.wait_ge(stored[b], LOAD * steps)

        @block.scalar
        def _(act):
            def first_part(t, b):
                act.wait_ge(loaded[b], (t + 1) * LOAD)
                act.wait_ge(turned[b], t)
                nc.scalar.activation(part(b, 0), raw[b][:, :, :, :], ACT.Copy).then_inc(first[b], 1)

            def second_part(t, b):
                act.wait_ge(rested[b], t + 1)
                nc.scalar.activation(part(b, 1), rest[b][:, :, :, :], ACT.Copy).then_inc(second[b], 1)

            def copy_out(t, b):
                act.wait_ge(turned[b], t + 1)
                act.wait_ge(stored[b], t * LOAD)
                nc.scalar.activation(out[b][:, 0:half], ps16[:, 4096 * b:4096 * b + half],
                                     ACT.Copy).then_inc(copied_a[b], 1)

            act.wait_ge(padded, 4)
            for b in range(2):
                first_part(0, b)
            with act.Fori(0, steps - 1) as t:
                for b in range(2):
                    second_part(t, b)
                for b in range(2):
                    first_part(t + 1, b)
                    copy_out(t, b)
            for b in range(2):
                second_part(steps - 1, b)
            for b in range(2):
                copy_out(steps - 1, b)

        @block.vector
        def _(dve):
            v = nc.vector

            def first_rest(t, b):
                dve.wait_ge(first[b], t + 1)
                dve.wait_ge(split[b], t)
                v.tensor_tensor(rest[b][:, :, :, :], raw[b][:, :, :, :], part(b, 0), ALU.subtract).then_inc(rested[b], 1)

            def third_part(t, b):
                dve.wait_ge(second[b], t + 1)
                v.tensor_tensor(part(b, 2), rest[b][:, :, :, :], part(b, 1), ALU.subtract).then_inc(split[b], 1)

            def copy_out(t, b):
                dve.wait_ge(turned[b], t + 1)
                dve.wait_ge(stored[b], t * LOAD)
                v.tensor_copy(out[b][:, half:NP], ps16[:, 4096 * b + half:4096 * b + NP]).then_inc(copied_v[b], 1)

            def lengths(t, b):
                dve.wait_ge(squared[b], t + 1)
                v.reduce_sum(norms[:, bass.ds(PREP * (2 * t + b), PREP), :].rearrange("p d i -> p (d i)"),
                             square[b][:, :, :], AX.X).then_inc(normed[b], 1)

            for b in range(2):
                v.memset(parts[b][:, :, :, SHIFT0:SHIFT0 + SPLITS], shift_row).then_inc(padded, 1)
                v.memset(parts[b][:, :, :, SHIFT0 + SPLITS:SROW], 0.0).then_inc(padded, 1)
            for b in range(2):
                first_rest(0, b)
            with dve.Fori(0, steps - 1) as t:
                for b in range(2):
                    third_part(t, b)
                for b in range(2):
                    lengths(t, b)
                for b in range(2):
                    first_rest(t + 1, b)
                    copy_out(t, b)
            for b in range(2):
                third_part(steps - 1, b)
            for b in range(2):
                copy_out(steps - 1, b)
                lengths(steps - 1, b)

        @block.gpsimd
        def _(pool):
            with pool.Fori(0, steps) as t:
                for b in range(2):
                    pool.wait_ge(loaded[b], (t + 1) * LOAD)
                    pool.wait_ge(normed[b], t)
                    raw_b = raw[b][:, :, :, :].rearrange("p d i h -> p (d i) h")
                    nc.gpsimd.tensor_tensor(square[b][:, :, :], raw_b, raw_b, ALU.mult).then_inc(squared[b], 1)

        @block.tensor
        def _(pe):
            pe.wait_ge(padded, 4)
            with pe.Fori(0, steps) as t:
                for b in range(2):
                    pe.wait_ge(split[b], t + 1)
                    pe.wait_ge(copied_a[b], t)
                    pe.wait_ge(copied_v[b], t)
                    for i in range(BLOCKS):
                        ins = nc.tensor.transpose(ps16[:, 4096 * b + P * i:4096 * b + P * (i + 1)],
                                                  parts[b][:, i, :, :].rearrange("p d r -> p (d r)"),
                                                  keep.ident16[:, :])
                    ins.then_inc(turned[b], 1)


def load_k(sp, k_tile, k_parts, d, sem):
    for a in range(SPLITS):
        sp.dma_start(k_tile[SROW * a:SROW * (a + 1), :], k_parts[d]).then_inc(sem, LOAD)


def load_q(sp, q_tile, q_parts, d, cols, sem):
    for a in range(SPLITS):
        for c in range(SPLITS):
            row = SROW * a + HEADS * c
            sp.dma_start(q_tile[row:row + HEADS, :], q_parts[d, HEADS * a:HEADS * (a + 1), cols]).then_inc(sem, LOAD)


def row_max_phase(nc, keep, adj, k_parts, q_parts, top):
    regular = adj[0:FULL].rearrange("(p i) m -> i p m", i=BLOCKS)
    last = adj[FULL:N].rearrange("(i p) m -> i p m", p=1)
    with ExitStack() as stack:
        mem = Memory(nc, stack)
        nat = mem.sb("max_nat", [P, NP])
        k_tile = [mem.sb(f"max_k{b}", [KROWS, NP], BF16) for b in range(2)]
        q_tile = [mem.sb(f"max_q{b}", [KROWS, P], BF16) for b in range(2)]
        junk = [mem.sb(f"max_junk{b}", [P, BANK]) for b in range(2)]
        segs = [mem.sb(f"max_segs{b}", [P, 8]) for b in range(2)]
        q_zeroed, loaded = mem.sem("max_q_zeroed"), mem.sems("max_loaded", 2)
        nat_loaded, nat_scaled = mem.sem("max_nat_loaded"), mem.sem("max_nat_scaled")
        scored, maxed = mem.sems("max_scored", 8), mem.sems("max_maxed", 8)
        topped = mem.sems("max_topped", 2)
        ps = keep.ps
        pairs = BATCHES // 2
        blocks_of = [(j, min(4, 24 - j)) for j in range(0, 24, 4)] + [(24, 1), (25, 1)]

        def cols_of(j):
            return N - P * (BLOCKS - 1) if j == BLOCKS - 1 else P

        block = stack.enter_context(nc.Block())

        @block.sync
        def _(sp):
            sp.wait_ge(q_zeroed, 3)
            with sp.Fori(0, BLOCKS) as i:
                for b in range(2):
                    sp.wait_ge(topped[b], i * pairs)
                sp.dma_start(nat[0:112, 0:N], regular[i, 0:112]).then_inc(nat_loaded, LOAD)
                sp.dma_start(nat[112:127, 0:N], regular[i, 112:127]).then_inc(nat_loaded, LOAD)
                last_row = nc.s_assert_within(FULL + i - i // (BLOCKS - 1), FULL, N - 1,
                                              skip_runtime_bounds_check_because="i // 25 is 1 for the last i alone")
                sp.dma_start(nat[127:P, 0:N], adj[bass.ds(last_row, 1)]).then_inc(nat_loaded, LOAD)
                with sp.Fori(0, pairs) as t:
                    for b in range(2):
                        sp.wait_ge(topped[b], i * pairs + t)
                        load_k(sp, k_tile[b], k_parts, 2 * t + b, loaded[b])
                        load_q(sp, q_tile[b], q_parts, 2 * t + b, bass.ds(i * P, P), loaded[b])

        @block.tensor
        def _(pe):
            with pe.Fori(0, BLOCKS) as i:
                with pe.Fori(0, pairs) as t:
                    for b in range(2):
                        pe.wait_ge(loaded[b], (i * pairs + t + 1) * (12 * LOAD))
                        for s, (j, n) in enumerate(blocks_of):
                            width = P * (n - 1) + cols_of(j + n - 1)
                            pe.wait_ge(maxed[s], i * BATCHES + 2 * t + b)
                            nc.tensor.matmul(ps[:, BANK * s:BANK * s + width], q_tile[b][:, :],
                                             k_tile[b][:, P * j:P * j + width],
                                             start=True, stop=True).then_inc(scored[s], 1)

        @block.gpsimd
        def _(pool):
            for b in range(2):
                nc.gpsimd.memset(q_tile[b][:, :], 0.0).then_inc(q_zeroed, 1)

        @block.scalar
        def _(act):
            act.wait_ge(q_zeroed, 3)
            with act.Fori(0, BLOCKS) as i:
                act.wait_ge(nat_loaded, (i + 1) * (3 * LOAD))
                nc.scalar.activation(nat[:, :], nat[:, :], ACT.Copy, scale=2.0 / SCALE).then_inc(nat_scaled, 1)

        @block.vector
        def _(dve):
            v = nc.vector
            v.memset(nat[:, N:NP], 0.0).then_inc(q_zeroed, 1)
            with dve.Fori(0, BLOCKS) as i:
                nat_blocks = nat[:, :].rearrange("p (q j) -> p j q", j=BLOCKS)
                with dve.Fori(0, pairs) as t:
                    for b in range(2):
                        count = i * BATCHES + 2 * t + b
                        ready = count + 1
                        scaled = i + 1
                        for value in (count, ready, scaled):
                            dve.compute_val(value)
                        for s, (j, n) in enumerate(blocks_of):
                            q = cols_of(j + n - 1)
                            dve.wait_ge(q_zeroed, 3)
                            if b == 0 and s == 0:
                                dve.wait_ge(nat_scaled, scaled)
                            dve.wait_ge(scored[s], ready)
                            if s >= 2:
                                dve.wait_ge(maxed[s - 2], ready)
                            elif s < 2:
                                dve.wait_ge(maxed[6 + s], count)
                            v.tensor_tensor_reduce(
                                out=junk[s % 2][:, 0:n * q].rearrange("p (j q) -> p j q", q=q),
                                in0=ps[:, BANK * s:BANK * s + n * q].rearrange("p (j q) -> p j q", q=q),
                                in1=nat_blocks[:, j:j + n, 0:q], scale=1.0, scalar=-3.0e38, op0=ALU.add,
                                op1=ALU.max, accum_out=segs[b][:, s:s + 1]).then_inc(maxed[s], 1)
                        for s in range(8):
                            dve.wait_ge(maxed[s], ready)
                        v.reduce_max(top[:, bass.ds(i, 1), bass.ds(2 * t + b, 1)].rearrange("p a d -> p (a d)"),
                                     segs[b][:, :], AX.X).then_inc(topped[b], 1)


def bound_phase(nc, keep, q_norms, k_norms, top, flag):
    with ExitStack() as stack:
        mem = Memory(nc, stack)
        k_top, k_all = mem.sb("b_k_top", [P, BATCHES]), mem.sb("b_k_all", [P, BATCHES])
        prod = mem.sb("b_prod", [P, BATCHES, BLOCKS])
        most, all_most = mem.sb("b_most", [P, 2]), mem.sb("b_all_most", [P, 2])
        small = mem.sb("b_small", [P, 2])
        k_topped, k_known, squared, rooted = (mem.sem("b_" + x) for x in ("k_topped", "k_known", "squared", "rooted"))
        mosts, most_known, chain = mem.sem("b_mosts"), mem.sem("b_most_known"), mem.sem("b_chain")
        block = stack.enter_context(nc.Block())

        @block.vector
        def _(dve):
            v = nc.vector
            link = Chain(dve, chain)
            v.reduce_max(k_top[:, :], k_norms[:, :, :], AX.X).then_inc(k_topped, 1)
            v.reduce_max(most[:, 1:2], keep.absmax[:, :], AX.X).then_inc(mosts, 1)
            dve.wait_ge(k_known, 1)
            v.tensor_tensor(prod[:, :, :], q_norms[:, :, :], bcast(k_all[:, :], BLOCKS), ALU.mult).then_inc(squared, 1)
            dve.wait_ge(rooted, 1)
            v.reduce_max(most[:, 0:1], prod[:, :, :].rearrange("p d i -> p (d i)"), AX.X).then_inc(mosts, 1)
            link(v.tensor_scalar(top[:, :, :].rearrange("p i d -> p d i"), prod[:, :, :], ROUND, HIGH / SCALE,
                                 ALU.mult, ALU.subtract))
            link(v.tensor_scalar(top[:, :, :], top[:, :, :], 0.0, None, ALU.max))
            dve.wait_ge(most_known, 1)
            link(v.tensor_scalar(small[:, 0:1], all_most[:, 0:1], BOUND / (SCALE * ROUND), None, ALU.is_le))
            link(v.tensor_scalar(small[:, 1:2], all_most[:, 1:2], ADJ_BOUND, None, ALU.is_le))
            link(v.tensor_tensor(small[:, 0:1], small[:, 0:1], small[:, 1:2], ALU.mult))
            link(v.tensor_copy(flag[:, :], small[:, 0:1]))

        @block.scalar
        def _(act):
            act.wait_ge(squared, 1)
            nc.scalar.activation(prod[:, :, :], prod[:, :, :], ACT.Sqrt).then_inc(rooted, 1)

        @block.gpsimd
        def _(pool):
            pool.wait_ge(k_topped, 1)
            nc.gpsimd.partition_all_reduce(k_all[:, :], k_top[:, :], P, bass.bass_isa.ReduceOp.max).then_inc(k_known, 1)
            pool.wait_ge(mosts, 2)
            nc.gpsimd.partition_all_reduce(all_most[:, :], most[:, :], P, bass.bass_isa.ReduceOp.max).then_inc(most_known, 1)


def shift_phase(nc, keep, top, q_parts):
    with ExitStack() as stack:
        mem = Memory(nc, stack)
        rest = mem.sb("s_rest", [P, BLOCKS, BATCHES])
        part = mem.sb("s_part", [P, BLOCKS, BATCHES], BF16)
        out = mem.sb("s_out", [P, NP], BF16)
        chain, part_ready, turned, copied, stored = (mem.sem("s_" + x) for x in (
            "chain", "part_ready", "turned", "copied", "stored"))
        ps16 = keep.ps[:, :].bitcast(BF16)
        block = stack.enter_context(nc.Block())

        @block.sync
        def _(sp):
            for s in range(SPLITS):
                sp.wait_ge(copied, s + 1)
                sp.dma_start(q_parts[:, SHIFT0 + s, :], out[:, :]).then_inc(stored, LOAD)
            sp.wait_ge(stored, SPLITS * LOAD)

        @block.tensor
        def _(pe):
            for s in range(SPLITS):
                pe.wait_ge(part_ready, s + 1)
                pe.wait_ge(copied, s)
                for i in range(BLOCKS):
                    ins = nc.tensor.transpose(ps16[:, P * i:P * (i + 1)], part[:, i, :], keep.ident16[:, :])
                ins.then_inc(turned, 1)

        @block.vector
        def _(dve):
            v = nc.vector
            link = Chain(dve, chain)
            link(v.tensor_scalar(rest[:, :, :], top[:, :, :], -1.0, None, ALU.mult))
            for s in range(SPLITS):
                dve.wait_ge(turned, s)
                v.tensor_copy(part[:, :, :], rest[:, :, :]).then_inc(part_ready, 1)
                dve.wait_ge(part_ready, s + 1)
                link(v.tensor_tensor(rest[:, :, :], rest[:, :, :], part[:, :, :], ALU.subtract))
                dve.wait_ge(turned, s + 1)
                dve.wait_ge(stored, s * LOAD)
                v.tensor_copy(out[:, :], ps16[:, 0:NP]).then_inc(copied, 1)


def attention_phase(nc, keep, group, pool_blocks, adj_t, k_parts, q_parts, v_flat, o_flat):
    first, chunks, nb = group
    width = nb * P
    acc_cols = nb * 32
    flat_t = adj_t.rearrange("i p j q -> i p (j q)")
    v_batches = bass.AP(v_flat.tensor, 0, [[VG * N, BATCHES], [VG * BLOCKS, P], [1, VG * BLOCKS]])
    o_batches = bass.AP(o_flat.tensor, 0, [[HEADS * N, BATCHES], [HEADS * BLOCKS, P], [1, HEADS * BLOCKS]])
    name = f"a{first}_{len(pool_blocks)}_"
    turns = BATCHES // 2
    units = 2 * BLOCKS
    by_pool = [j in pool_blocks for j in range(BLOCKS)]
    n_pool = len(pool_blocks)
    n_dve = BLOCKS - n_pool
    pool_rank = [sum(by_pool[:j]) for j in range(BLOCKS)]
    dve_rank = [j - pool_rank[j] for j in range(BLOCKS)]
    rows_of = [P] * (BLOCKS - 1) + [N - P * (BLOCKS - 1)]
    if n_pool:
        alone = [(j,) for j in range(BLOCKS) if not any(abs(j - p) <= 1 for p in pool_blocks)]
        sets = sorted([(p - 1, p + 1) for p in pool_blocks] + alone)
    else:
        sets = [(j, j + 1) for j in range(0, BLOCKS, 2)]
    n_sets = len(sets)
    part_of = [n for n, (begin, end) in enumerate(ADJ_PARTS) for _ in range(begin, end)]
    set_of = {j: n for n, js in enumerate(sets) for j in js}
    ahead_by, ring, pool_slots = (4, 4, 4) if n_pool else (2, 2, 0)

    def weighed_at(k):
        b, j = divmod(k, BLOCKS)
        return b * BLOCKS + (min(j + POOL_LAG, BLOCKS - 1) if by_pool[j] else sets[set_of[j]][-1])

    weigh_at = [[k for k in range(units) if weighed_at(k) == at] for at in range(units)]
    first_weighed, *_, last_weighed = (k for ks in weigh_at[:BLOCKS] for k in ks)
    with ExitStack() as stack:
        mem = Memory(nc, stack)
        adj_c = mem.sb(name + "adj", [P, nb, BLOCKS, P])
        k_tile = [mem.sb(f"{name}k{b}", [KROWS, NP], BF16) for b in range(2)]
        q_tile = [mem.sb(f"{name}q{b}", [KROWS, width], BF16) for b in range(2)]
        v_tile = [mem.sb(f"{name}v{b}", [P, BLOCKS, VG]) for b in range(2)]
        dve_ring = mem.sb(name + "probs", [P, ring, 2, nb, P])
        pool_ring = [mem.sb(f"{name}pool_probs{b}", [P, nb, P]) for b in range(pool_slots)]
        turned = mem.sb(name + "turned", [P, nb, 32])
        inv = mem.sb(name + "inv", [P, nb])
        o_tile = [mem.sb(f"{name}o{b}", [P, nb, HEADS]) for b in range(2)]
        adj_loaded = mem.sems(name + "adj_loaded", len(ADJ_PARTS))
        loaded, cleared = mem.sems(name + "loaded", 2), mem.sem(name + "cleared")
        factored, scores_ready, added, sums_exped, scores_exped, multiplied, batch_summed = (mem.sem(name + x) for x in (
            "factored", "scores_ready", "added", "sums_exped", "scores_exped", "multiplied", "batch_summed"))
        acc_read, inverted, out_ready, stored = (mem.sem(name + x) for x in (
            "acc_read", "inverted", "out_ready", "stored"))
        ps = keep.ps
        per_load = (SPLITS + SPLITS * SPLITS + 2) * LOAD
        acc = [ps[:, BANK * (2 * SBUFS + b):BANK * (2 * SBUFS + b) + acc_cols] for b in range(2)]

        def score(j):
            at = 2 * BANK * (j % SBUFS)
            return ps[:, at:at + width]

        def set_slot(k):
            b, j = divmod(k, BLOCKS)
            return (b * n_sets + set_of[j]) % ring

        def probs(k):
            b, j = divmod(k, BLOCKS)
            return pool_ring[(b * n_pool + pool_rank[j]) % pool_slots] if by_pool[j] else \
                dve_ring[:, set_slot(k), sets[set_of[j]].index(j)]

        block = stack.enter_context(nc.Block())

        @block.sync
        def _(sp):
            def load(d, b, cols):
                load_k(sp, k_tile[b], k_parts, d, loaded[b])
                load_q(sp, q_tile[b], q_parts, d, cols, loaded[b])
                sp.dma_start(q_tile[b][SHIFT0:SROW, :], q_parts[d, SHIFT0:SROW, cols]).then_inc(loaded[b], LOAD)
                sp.dma_start(v_tile[b][:, :, :].rearrange("p j h -> p (j h)"), v_batches[d]).then_inc(loaded[b], LOAD)

            def load_adj(c, part):
                begin, end = ADJ_PARTS[part]
                for i in range(nb):
                    sp.dma_start(adj_c[:, i, begin:end, :].rearrange("p j q -> p (j q)"),
                                 flat_t[first + c * nb + i][:, P * begin:P * end]).then_inc(adj_loaded[part], LOAD)

            def store(ready, d, b, c):
                sp.wait_ge(out_ready, ready)
                sp.dma_start(o_batches[d, :, bass.ds((first + c * nb) * HEADS, nb * HEADS)],
                             o_tile[b][:, :, :].rearrange("p i h -> p (i h)")).then_inc(stored, LOAD)

            sp.wait_ge(cleared, 3)
            with sp.Fori(0, chunks) as c:
                cols = bass.ds((first + c * nb) * P, width)
                done = c * BATCHES
                stores = done * LOAD
                for value in (done, stores, done * n_dve, done * n_pool):
                    sp.compute_val(value)
                sp.wait_ge(added, done * n_dve)
                sp.wait_ge(multiplied, done * n_pool)
                load_adj(c, 0)
                sp.wait_ge(batch_summed, done)
                sp.wait_ge(stored, stores)
                load(0, 0, cols)
                for part in range(1, len(ADJ_PARTS)):
                    load_adj(c, part)
                load(1, 1, cols)
                with sp.Fori(0, turns - 1) as t:
                    for b in range(2):
                        d = 2 * t + b
                        stores, used, ready = (done + d) * LOAD, done + d + 1, done + c + d + 2
                        for value in (stores, used, ready):
                            sp.compute_val(value)
                        sp.wait_ge(stored, stores)
                        sp.wait_ge(batch_summed, used)
                        load(d + 2, b, cols)
                        store(ready, d, b, c)
                for b in range(2):
                    d = BATCHES - 2 + b
                    stores, ready = (done + d) * LOAD, done + c + d + 2
                    for value in (stores, ready):
                        sp.compute_val(value)
                    sp.wait_ge(stored, stores)
                    store(ready, d, b, c)
            sp.wait_ge(stored, chunks * BATCHES * LOAD)

        @block.tensor
        def _(pe):
            def scores(k, batch):
                b, j = k // BLOCKS, k % BLOCKS
                before, of = (j - SBUFS, b) if j >= SBUFS else (BLOCKS - 1 - (BLOCKS - 1 - j) % SBUFS, b - 1)
                if of >= 0:
                    if by_pool[before]:
                        pe.wait_ge(scores_exped, (batch + of) * n_pool + (pool_rank[before] + 1))
                    else:
                        pe.wait_ge(added, (batch + of) * n_dve + (dve_rank[before] + 1))
                at, kt, qt = 2 * BANK * (j % SBUFS), k_tile[b % 2], q_tile[b % 2]
                for lo in range(0, width, BANK):
                    hi = min(lo + BANK, width)
                    ins = nc.tensor.matmul(ps[:, at + lo:at + hi], kt[:, P * j:P * (j + 1)], qt[:, lo:hi],
                                           start=True, stop=True)
                ins.then_inc(scores_ready, 1)

            def weigh(k, batch, c):
                b, j = divmod(k, BLOCKS)
                if by_pool[j]:
                    pe.wait_ge(multiplied, (batch + b) * n_pool + (pool_rank[j] + 1))
                else:
                    pe.wait_ge(sums_exped, (batch + b) * n_sets + (set_of[j] + 1))
                if j == first_weighed:
                    pe.wait_ge(acc_read, batch + c + b)
                for g in range(4):
                    ins = nc.tensor.matmul(acc[b][32 * g:32 * g + VG, :], v_tile[b][0:rows_of[j], j, :],
                                           probs(k)[0:rows_of[j], :, 32 * g:32 * (g + 1)],
                                           start=j == first_weighed, stop=j == last_weighed)
                if j == last_weighed:
                    ins.then_inc(batch_summed, 1)

            def turn(batch, pair, c, final):
                for k in range(units):
                    ahead = k + ahead_by
                    if ahead < units or not final:
                        if ahead == BLOCKS:
                            pe.wait_ge(loaded[1], (pair + 1) * per_load)
                        if ahead == units:
                            pe.wait_ge(loaded[0], (pair + 2) * per_load)
                        scores(ahead, batch)
                    for u in weigh_at[k]:
                        weigh(u, batch, c)

            pe.wait_ge(cleared, 3)
            with pe.Fori(0, chunks) as c:
                pe.wait_ge(loaded[0], (c * turns + 1) * per_load)
                for k in range(ahead_by):
                    scores(k, c * BATCHES)
                with pe.Fori(0, turns - 1) as t:
                    turn((c * turns + t) * 2, c * turns + t, c, False)
                turn(c * BATCHES + (BATCHES - 2), c * turns + (turns - 1), c, True)

        @block.scalar
        def _(act):
            def turn(c, t, factors):
                for k in range(units):
                    b, j = divmod(k, BLOCKS)
                    batch = (c * turns + t) * 2 + b
                    if by_pool[j]:
                        if factors and b == 0:
                            act.wait_ge(adj_loaded[part_of[j]], (c + 1) * (nb * LOAD))
                            nc.scalar.activation(adj_c[:, :, j, :], adj_c[:, :, j, :], ACT.Exp, scale=2.0
                                                 ).then_inc(factored, 1)
                        act.wait_ge(scores_ready, batch * BLOCKS + (j + 1))
                        nc.scalar.activation(probs(k)[:, :, :].rearrange("p i q -> p (i q)"), score(j), ACT.Exp,
                                             scale=SCALE).then_inc(scores_exped, 1)
                    elif j == sets[set_of[j]][-1]:
                        act.wait_ge(added, batch * n_dve + (dve_rank[j] + 1))
                        tiles = dve_ring[:, set_slot(k), 0:len(sets[set_of[j]])].rearrange("p s i q -> p (s i q)")
                        nc.scalar.activation(tiles, tiles, ACT.Exp, scale=2.0).then_inc(sums_exped, 1)

            with act.Fori(0, chunks) as c:
                turn(c, 0, True)
                with act.Fori(1, turns) as t:
                    turn(c, t, False)

        @block.gpsimd
        def _(pool):
            for b in range(2):
                nc.gpsimd.memset(q_tile[b][:, :], 0.0).then_inc(cleared, 1)
            if n_pool:
                with pool.Fori(0, chunks) as c:
                    with pool.Fori(0, turns) as t:
                        for k in range(units):
                            b, j = divmod(k, BLOCKS)
                            if by_pool[j]:
                                if b == 0:
                                    pool.wait_ge(factored, c * n_pool + (pool_rank[j] + 1))
                                pool.wait_ge(scores_exped, ((c * turns + t) * 2 + b) * n_pool + (pool_rank[j] + 1))
                                nc.gpsimd.tensor_tensor(probs(k)[:, :, :], probs(k)[:, :, :], adj_c[:, :, j, :],
                                                        ALU.mult).then_inc(multiplied, 1)

        @block.vector
        def _(dve):
            v = nc.vector

            def finish(b, done, before):
                dve.wait_ge(batch_summed, done)
                v.transpose(turned[:, :, :].rearrange("p i c -> p (i c)"), acc[b]).then_inc(acc_read, 1)
                dve.wait_ge(acc_read, before + 1)
                v.reciprocal(inv[:, :], turned[:, :, HEADS:VG].rearrange("p i a -> p (i a)")).then_inc(inverted, 1)
                dve.wait_ge(inverted, before + 1)
                v.tensor_tensor(o_tile[b][:, :, :], turned[:, :, 0:HEADS], bcast(inv[:, :], HEADS),
                                ALU.mult).then_inc(out_ready, 1)
                dve.wait_ge(out_ready, before + 1)

            v.memset(ps[:, BANK * 2 * SBUFS:], 1.0).then_inc(cleared, 1)
            dve.wait_ge(cleared, 3)
            with dve.Fori(0, chunks) as c:
                with dve.Fori(0, turns) as t:
                    for k in range(units):
                        b, j = divmod(k, BLOCKS)
                        batch = (c * turns + t) * 2 + b
                        if b == 0 and (j == 0 or part_of[j] > part_of[j - 1]):
                            dve.wait_ge(adj_loaded[part_of[j]], (c + 1) * (nb * LOAD))
                        if not by_pool[j]:
                            dve.wait_ge(scores_ready, batch * BLOCKS + (j + 1))
                            v.scalar_tensor_tensor(
                                out=probs(k), in0=score(j).rearrange("p (i q) -> p i q", q=P),
                                scalar=SCALE / 2, in1=adj_c[:, :, j, :], op0=ALU.mult, op1=ALU.add
                            ).then_inc(added, 1)
                        if j == FINISH_AT:
                            finish(1 - b, batch, batch + c)
                dve.wait_ge(stored, ((c + 1) * BATCHES - 2) * LOAD)
                finish(1, (c + 1) * BATCHES, (c + 1) * BATCHES + c)


def output_phase(nc, keep, wo, o_flat):
    x = keep.x
    chunks = QCOLS // P
    rows = o_flat.rearrange("(p i c) -> i p c", i=BLOCKS, c=QCOLS)
    with ExitStack() as stack:
        mem = Memory(nc, stack)
        w = mem.sb("wo", [P, chunks, P])
        w_t = mem.sb("wo_t", [P, chunks, F])
        o = [mem.sb(f"o_rows{b}", [P, chunks, P]) for b in range(2)]
        o_t = [mem.sb(f"o_t{b}", [P, chunks, P]) for b in range(2)]
        sq = mem.sb("wo_sq", [P, BLOCKS, F])
        norm = Norm(mem, "wo")
        w_loaded, w_turned, w_copied = mem.sem("wo_loaded"), mem.sem("wo_turned"), mem.sem("wo_copied")
        loaded, turned, copied = mem.sems("o_loaded", 2), mem.sems("o_turned", 2), mem.sems("o_copied", 2)
        projected, added = mem.sems("o_projected", 2), mem.sems("o_added", 2)
        chain = mem.sem("wo_chain")
        ps = keep.ps
        block = stack.enter_context(nc.Block())

        @block.sync
        def _(sp):
            sp.dma_start(w[:, :, :].rearrange("p c k -> p (c k)"), wo).then_inc(w_loaded, LOAD)
            with sp.Fori(0, BLOCKS // 2) as t:
                for b in range(2):
                    sp.wait_ge(turned[b], t)
                    sp.dma_start(o[b][:, :, :].rearrange("p c k -> p (c k)"), rows[2 * t + b]).then_inc(loaded[b], LOAD)

        @block.tensor
        def _(pe):
            pe.wait_ge(w_loaded, LOAD)
            for c in range(chunks):
                ins = nc.tensor.transpose(ps[:, P * c:P * (c + 1)], w[:, c, :], keep.ident[:, :])
            ins.then_inc(w_turned, 1)
            pe.wait_ge(w_copied, 1)
            with pe.Fori(0, BLOCKS // 2) as t:
                for b in range(2):
                    pe.wait_ge(loaded[b], (t + 1) * LOAD)
                    pe.wait_ge(copied[b], t)
                    for c in range(chunks):
                        at = QCOLS * b + P * c
                        ins = nc.tensor.transpose(ps[:, at:at + P], o[b][:, c, :], keep.ident[:, :])
                    ins.then_inc(turned[b], 1)
                for b in range(2):
                    pe.wait_ge(copied[b], t + 1)
                    pe.wait_ge(added[b], t)
                    at = BANK * (4 + b)
                    for c in range(chunks):
                        ins = nc.tensor.matmul(ps[:, at:at + F], o_t[b][:, c, :], w_t[:, c, :],
                                               start=c == 0, stop=c == chunks - 1)
                    ins.then_inc(projected[b], 1)

        @block.scalar
        def _(act):
            act.wait_ge(w_copied, 1)
            with act.Fori(0, BLOCKS // 2) as t:
                for b in range(2):
                    act.wait_ge(turned[b], t + 1)
                    act.wait_ge(projected[b], t)
                    nc.scalar.activation(o_t[b][:, :, :].rearrange("p c k -> p (c k)"),
                                         ps[:, QCOLS * b:QCOLS * (b + 1)], ACT.Copy).then_inc(copied[b], 1)
            layer_norm_root(nc, act, norm)

        @block.vector
        def _(dve):
            dve.wait_ge(w_turned, 1)
            nc.vector.tensor_copy(w_t[:, :, :].rearrange("p c f -> p (c f)"), ps[:, 0:QCOLS]).then_inc(w_copied, 1)
            with dve.Fori(0, BLOCKS // 2) as t:
                for b in range(2):
                    x_i = x[:, bass.ds(2 * t + b, 1), :].rearrange("p a f -> p (a f)")
                    dve.wait_ge(projected[b], t + 1)
                    nc.vector.tensor_tensor(x_i, ps[:, BANK * (4 + b):BANK * (4 + b) + F], x_i,
                                            ALU.add).then_inc(added[b], 1)
            for b in range(2):
                dve.wait_ge(added[b], BLOCKS // 2)
            layer_norm(nc, dve, Chain(dve, chain), x, sq, norm)


def edge_phase(nc, keep, adj, weight, out):
    regular = adj[0:FULL].rearrange("(p i) m -> i p m", i=BLOCKS)
    last = adj[FULL:N].rearrange("(i p) m -> i p m", p=1)
    x = keep.x
    with ExitStack() as stack:
        mem = Memory(nc, stack)
        w, w_t = mem.sb("e_w", [P, F]), mem.sb("e_w_t", [P, F])
        x_t = mem.sb("e_x_t", [P, NP])
        h = mem.sb("e_h", [P, BLOCKS, F])
        dst = mem.sb("e_dst", [P, NP])
        att = mem.sb("e_att", [P, P])
        src = mem.sb("e_src", [P, BLOCKS])
        nat = [mem.sb(f"e_nat{b}", [P, NP]) for b in range(2)]
        edge = [mem.sb(f"e_edge{b}", [P, NP]) for b in range(2)]
        tau = [mem.sb(f"e_tau{b}", [P, NP]) for b in range(2)]
        both = [mem.sb(f"e_both{b}", [P, NP]) for b in range(2)]
        sq = both[0][:, :].rearrange("p (i f) -> p i f", f=F)
        h_t = both[1]
        z_t = tau[0]
        h_j = [mem.sb(f"e_h_j{b}", [P, F]) for b in range(2)]
        den_of = mem.sb("e_den_of", [P, NP])
        den = mem.sb("e_den", [P, BLOCKS])
        norm = Norm(mem, "e")
        w_loaded, x_turned, w_turned, x_copied = (mem.sem("e_" + s) for s in (
            "w_loaded", "x_turned", "w_turned", "x_copied"))
        h_done, h_copied, ht_done, ht_copied, dst_done, dst_copied = (mem.sem("e_" + s) for s in (
            "h_done", "h_copied", "ht_done", "ht_copied", "dst_done", "dst_copied"))
        padded, chain, src_ready = mem.sem("e_padded"), mem.sem("e_chain"), mem.sem("e_src_ready")
        loaded, summed, leaky, exped, h_set = (mem.sems("e_" + s, 2) for s in (
            "loaded", "summed", "leaky", "exped", "h_set"))
        z_copied, z_turned = mem.sem("e_z_copied"), mem.sem("e_z_turned")
        den_added, den_summed = mem.sem("e_den_added"), mem.sem("e_den_summed")
        tau_ready, both_ready, weighed = (mem.sems("e_" + s, 2) for s in ("tau_ready", "both_ready", "weighed"))
        out_stored = mem.sem("e_out_stored")
        ps = keep.ps
        den_col = 7 * BANK
        w_ps = ps[:, den_col:den_col + F]
        last_rows = P - 1
        pairs = BLOCKS // 2
        block = stack.enter_context(nc.Block())

        @block.sync
        def _(sp):
            sp.dma_start(w[:, :], weight).then_inc(w_loaded, LOAD)

            def load(t, b, whole=True):
                i = 2 * t + b
                sp.wait_ge(both_ready[b], t)
                sp.dma_start(nat[b][0:112, 0:N], regular[i, 0:112]).then_inc(loaded[b], LOAD)
                sp.dma_start(nat[b][112:127, 0:N], regular[i, 112:127]).then_inc(loaded[b], LOAD)
                if whole:
                    sp.dma_start(nat[b][127:P, 0:N], last[i]).then_inc(loaded[b], LOAD)

            with sp.Fori(0, pairs - 1) as t:
                for b in range(2):
                    load(t, b)
            load(pairs - 1, 0)
            load(pairs - 1, 1, whole=False)
            rows = out[0:FULL].rearrange("(p i) f -> p i f", i=BLOCKS)
            sp.wait_ge(norm.done, 1)
            sp.dma_start(rows[0:112], x[0:112]).then_inc(out_stored, LOAD)
            sp.dma_start(rows[112:127], x[112:127]).then_inc(out_stored, LOAD)
            sp.dma_start(out[FULL:N].rearrange("(p i) f -> p i f", p=1), x[127:P, 0:BLOCKS - 1]
                         ).then_inc(out_stored, LOAD)
            sp.wait_ge(out_stored, 3 * LOAD)

        @block.tensor
        def _(pe):
            def columns(lhs, rhs, sem):
                for at in range(0, NP, BANK):
                    end = min(at + BANK, NP)
                    ins = nc.tensor.matmul(ps[:, at:end], lhs, rhs[:, at:end], start=True, stop=True)
                ins.then_inc(sem, 1)

            for i in range(BLOCKS):
                ins = nc.tensor.transpose(ps[:, P * i:P * (i + 1)], x[:, i, :], keep.ident[:, :])
            ins.then_inc(x_turned, 1)
            pe.wait_ge(w_loaded, LOAD)
            nc.tensor.transpose(w_ps, w[:, :], keep.ident[:, :]).then_inc(w_turned, 1)
            pe.wait_ge(x_copied, 3)
            for i in range(BLOCKS):
                ins = nc.tensor.matmul(ps[:, P * i:P * (i + 1)], x_t[:, P * i:P * (i + 1)], w_t[:, :],
                                       start=True, stop=True)
            ins.then_inc(h_done, 1)
            pe.wait_ge(h_copied, 1)
            columns(w_t[:, :], x_t, ht_done)
            pe.wait_ge(ht_copied, 1)
            columns(att[:, :], h_t, dst_done)
            pe.wait_ge(dst_copied, 1)

            def numerators(t, b, rows, begin, end):
                pe.wait_ge(h_set[b], t + 1)
                pe.wait_ge(both_ready[b], t + 1)
                for at in range(0, NP, BANK):
                    to = min(at + BANK, NP)
                    ins = nc.tensor.matmul(ps[:, at:to], h_j[b][0:rows, :], both[b][0:rows, at:to],
                                           start=begin, stop=end, skip_group_check=True)
                ins.then_inc(weighed[b], 1)

            numerators(0, 0, P, True, False)
            numerators(0, 1, P, False, False)
            with pe.Fori(1, pairs - 1) as t:
                for b in range(2):
                    numerators(t, b, P, False, False)
            numerators(pairs - 1, 0, P, False, False)
            numerators(pairs - 1, 1, last_rows, False, True)
            pe.wait_ge(den_added, BLOCKS)
            for i in range(BLOCKS):
                ins = nc.tensor.matmul(ps[:, den_col + i:den_col + i + 1], den_of[:, P * i:P * (i + 1)],
                                       keep.ones[:, :], start=True, stop=True)
            ins.then_inc(den_summed, 1)
            pe.wait_ge(z_copied, 1)
            for i in range(BLOCKS):
                ins = nc.tensor.transpose(ps[:, P * i:P * (i + 1)], z_t[:, P * i:P * (i + 1)], keep.ident[:, :])
            ins.then_inc(z_turned, 1)

        @block.scalar
        def _(act):
            act.wait_ge(dst_copied, 1)
            act.wait_ge(src_ready, 1)

            def logits(t, b):
                act.wait_ge(tau_ready[b], t)
                nc.scalar.activation(edge[b][:, :], dst[:, :], ACT.Identity,
                                     bias=src[:, bass.ds(2 * t + b, 1)]).then_inc(summed[b], 1)

            def edges(t, b):
                act.wait_ge(leaky[b], t + 1)
                nc.scalar.activation(edge[b][:, :], edge[b][:, :], ACT.Exp).then_inc(exped[b], 1)

            def h_block(t, b):
                act.wait_ge(weighed[b], t)
                nc.scalar.activation(h_j[b][:, :], h[:, bass.ds(2 * t + b, 1), :].rearrange("p a f -> p (a f)"),
                                     ACT.Copy).then_inc(h_set[b], 1)

            def both_of(step, t):
                for b in range(2):
                    step(t, b)

            both_of(logits, 0)
            with act.Fori(0, pairs - 1) as t:
                both_of(edges, t)
                both_of(logits, t + 1)
                both_of(h_block, t)
            both_of(edges, pairs - 1)
            both_of(h_block, pairs - 1)
            layer_norm_root(nc, act, norm)

        def nat_blocks(b, rows):
            return nat[b][0:rows, :].rearrange("p (q i) -> p i q", i=BLOCKS)

        def as_blocks(tile, rows):
            return tile[0:rows, :].rearrange("p (i q) -> p i q", q=P)

        @block.gpsimd
        def _(pool):
            def square(t, b, rows):
                pool.wait_ge(tau_ready[b], t + 1)
                pool.wait_ge(weighed[b], t)
                nc.gpsimd.tensor_tensor(as_blocks(both[b], rows), as_blocks(tau[b], rows), nat_blocks(b, rows),
                                        ALU.mult).then_inc(both_ready[b], 1)

            with pool.Fori(0, pairs - 1) as t:
                for b in range(2):
                    square(t, b, P)
            square(pairs - 1, 0, P)
            square(pairs - 1, 1, last_rows)

        @block.vector
        def _(dve):
            v = nc.vector
            link = Chain(dve, chain)
            for b in range(2):
                v.memset(nat[b][:, N:NP], 1.0).then_inc(padded, 1)
            v.memset(den_of[:, :], 0.0).then_inc(padded, 1)
            dve.wait_ge(x_turned, 1)
            v.tensor_copy(x_t[:, :], ps[:, 0:NP]).then_inc(x_copied, 1)
            dve.wait_ge(w_turned, 1)
            v.tensor_copy(w_t[:, :], w_ps).then_inc(x_copied, 1)
            v.tensor_copy(att[:, :], keep.att_dst[:, :].to_broadcast([P, P])).then_inc(x_copied, 1)
            dve.wait_ge(h_done, 1)
            v.tensor_copy(h[:, :, :].rearrange("p i f -> p (i f)"), ps[:, 0:NP]).then_inc(h_copied, 1)
            dve.wait_ge(h_copied, 1)
            link(v.tensor_tensor(sq, h[:, :, :], keep.att_src[:, :].unsqueeze(1).to_broadcast([P, BLOCKS, F]),
                                 ALU.mult))
            v.reduce_sum(src[:, :], sq, AX.X).then_inc(src_ready, 1)
            dve.wait_ge(ht_done, 1)
            v.tensor_copy(h_t[:, :], ps[:, 0:NP]).then_inc(ht_copied, 1)
            dve.wait_ge(dst_done, 1)
            v.tensor_copy(dst[:, :], ps[:, 0:NP]).then_inc(dst_copied, 1)
            dve.wait_ge(src_ready, 1)
            dve.wait_ge(padded, 3)

            def weights(t, b, rows, loads):
                dve.wait_ge(exped[b], t + 1)
                dve.wait_ge(loaded[b], loads)
                dve.wait_ge(both_ready[b], t)
                v.tensor_tensor(as_blocks(tau[b], rows), as_blocks(edge[b], rows), nat_blocks(b, rows),
                                ALU.mult).then_inc(tau_ready[b], 1)
                dve.wait_ge(tau_ready[b], t + 1)
                dve.wait_ge(den_added, 2 * t + b)
                v.tensor_tensor(den_of[0:rows, :], den_of[0:rows, :], tau[b][0:rows, :], ALU.add).then_inc(den_added, 1)

            def leak(t, b):
                dve.wait_ge(summed[b], t + 1)
                v.scalar_tensor_tensor(out=edge[b][:, :], in0=edge[b][:, :], scalar=0.2, in1=edge[b][:, :],
                                       op0=ALU.mult, op1=ALU.max).then_inc(leaky[b], 1)

            with dve.Fori(0, pairs - 1) as t:
                for b in range(2):
                    leak(t, b)
                for b in range(2):
                    weights(t, b, P, (t + 1) * (3 * LOAD))
            for b in range(2):
                leak(pairs - 1, b)
            weights(pairs - 1, 0, P, pairs * 3 * LOAD)
            weights(pairs - 1, 1, last_rows, pairs * 3 * LOAD - LOAD)
            for b in range(2):
                dve.wait_ge(weighed[b], pairs)
            v.tensor_copy(z_t[:, :], ps[:, 0:NP]).then_inc(z_copied, 1)
            dve.wait_ge(den_summed, 1)
            link(v.reciprocal(den[:, :], ps[:, den_col:den_col + BLOCKS]))
            dve.wait_ge(z_turned, 1)
            z = ps[:, 0:NP].rearrange("p (i f) -> p i f", f=F)
            link(v.tensor_tensor(sq, z, bcast(den[:, :], F), ALU.mult))
            link(v.tensor_tensor(x[:, :, :], sq, x[:, :, :], ALU.add))
            layer_norm(nc, dve, link, x, sq, norm)


class Kept:

    def __init__(self, mem):
        self.ps = mem.stack.enter_context(mem.nc.psum_tensor("ps", [P, 8 * BANK], F32))
        self.x = mem.sb("x", [P, BLOCKS, F])
        self.ident, self.ident16 = mem.sb("ident", [P, P]), mem.sb("ident16", [P, P], BF16)
        self.ones = mem.sb("ones", [P, 1])
        self.bias0, self.bias2 = mem.sb("bias0", [P, F]), mem.sb("bias2", [P, F])
        self.att_src, self.att_dst = mem.sb("att_src", [P, F]), mem.sb("att_dst", [P, 1])
        self.rowsum, self.absmax = mem.sb("rowsum", [P, BLOCKS]), mem.sb("absmax", [P, BLOCKS])
        self.deg0, self.deg2 = mem.sb("deg0", [P, BLOCKS]), mem.sb("deg2", [P, BLOCKS])


def program(nc, x, adj, w0, b0, wq, wk, wv, wo, w2, b2, w3, att_src, att_dst, out):
    def scratch(name, shape, dt=F32):
        return nc.dram_tensor(name, shape, dt).ap()

    adj_t = scratch("adj_t", (BLOCKS, P, BLOCKS, P))
    q_flat, k_flat = scratch("q_flat", (NP * QCOLS,)), scratch("k_flat", (NP * QCOLS,))
    v_flat, o_flat = scratch("v_flat", (NP * QGROUPS * VG,)), scratch("o_flat", (NP * QCOLS,))
    q_parts = scratch("q_parts", (BATCHES, SROW, NP), BF16)
    k_parts = scratch("k_parts", (BATCHES, SROW, NP), BF16)
    with ExitStack() as stack:
        keep = Kept(Memory(nc, stack))
        setup_phase(nc, keep, x, b0, b2, att_src, att_dst, o_flat)
        adjacency_phase(nc, keep, adj, adj_t)
        gcn_phase(nc, keep, adj_t, w0, keep.deg0, keep.bias0, True)
        qkv_phase(nc, keep, wq, wk, wv, q_flat, k_flat, v_flat)
        with ExitStack() as bound_stack:
            mem = Memory(nc, bound_stack)
            top = mem.sb("top", [P, BLOCKS, BATCHES])
            flag = mem.sb("flag", [P, 1], mybir.dt.int32)
            with ExitStack() as norm_stack:
                mem = Memory(nc, norm_stack)
                k_norms, q_norms = (mem.sb(x, [P, BATCHES, BLOCKS]) for x in ("k_norms", "q_norms"))
                split_phase(nc, keep, k_flat, k_parts, k_norms, "sk_", 1.0)
                split_phase(nc, keep, q_flat, q_parts, q_norms, "sq_", 0.0)
                bound_phase(nc, keep, q_norms, k_norms, top, flag)
            bounded = nc.values_load(flag[0:1, 0:1], min_val=0, max_val=1)
            with nc.If(bounded < 1):
                row_max_phase(nc, keep, adj, k_parts, q_parts, top)
            shift_phase(nc, keep, top, q_parts)
        with nc.If(bounded < 1):
            for group in reversed(CHUNK_GROUPS):
                attention_phase(nc, keep, group, (), adj_t, k_parts, q_parts, v_flat, o_flat)
        with nc.Else():
            for group in reversed(CHUNK_GROUPS):
                attention_phase(nc, keep, group, POOL_BLOCKS, adj_t, k_parts, q_parts, v_flat, o_flat)
        output_phase(nc, keep, wo, o_flat)
        gcn_phase(nc, keep, adj_t, w2, keep.deg2, keep.bias2, False)
        edge_phase(nc, keep, adj, w3, out)


INPUTS = ("x", "adj", "L0_gnn_W", "L0_gnn_b", "L1_gnn_Wq", "L1_gnn_Wk", "L1_gnn_Wv", "L1_gnn_Wo", "L2_gnn_W",
          "L2_gnn_b", "L3_gnn_weight", "L3_gnn_att_src", "L3_gnn_att_dst")


def kernel(**inputs):
    import numpy as np
    import concourse.bacc as bacc
    from concourse.bass_utils import run_bass_kernel_spmd

    nc = bacc.Bacc("TRN2", target_bir_lowering=False, num_devices=1)
    arrays, args = {}, []
    for name in INPUTS:
        a = np.ascontiguousarray(inputs[name])
        arrays["in_" + name] = a
        args.append(nc.dram_tensor("in_" + name, a.shape, mybir.dt.from_np(a.dtype), kind="ExternalInput").ap())
    args.append(nc.dram_tensor("out", (N, F), F32, kind="ExternalOutput").ap())
    program(nc, *args)
    result = run_bass_kernel_spmd(nc, [arrays], core_ids=[0])
    return result.results[0]["out"]
```
